# Optimizing a Trainium2 kernel written in Bass

```python
import numpy as np
import jax
import jax.numpy as jnp

def _softmax(x, axis=-1):
    return jax.nn.softmax(x, axis=axis)

def _gelu(x):
    return jax.nn.gelu(x, approximate=True)

def _silu(x):
    return jax.nn.silu(x)

def _sigmoid(x):
    return jax.nn.sigmoid(x)

def _layernorm(x, axis=-1, eps=1e-05):
    m = jnp.mean(x, axis=axis, keepdims=True)
    v = jnp.var(x, axis=axis, keepdims=True)
    return (x - m) / jnp.sqrt(v + eps)

def _scatter_add(tgt, idx, src, axis=0):
    return tgt.at[idx].add(src)

def _segment_sum(src, seg, n):
    return jax.ops.segment_sum(src, seg, n)
kernel_name = 'mk_dlrm_tower_d1_rec_r8_2e50d0'

def setup_inputs(seed: int=0):
    np.random.seed(seed)
    _w = jnp.asarray

    def _rec_inputs():
        import jax
        import jax.numpy as jnp
        _tk = jax.random.key(seed)
        dense_ctx = jax.random.normal(jax.random.fold_in(_tk, 190), (2048, 16), jnp.float32)
        ids = jnp.stack([jax.random.randint(jax.random.fold_in(_tk, 200 + f), (2048,), 0, v, jnp.int32) for f, v in enumerate([1250, 12500, 1000, 1000, 1250, 1250, 1000, 1000, 1000, 125000, 12500, 12500, 1000, 12500, 1250, 12500, 1000, 1250, 1250, 1000, 12500, 1250, 1000, 12500, 1000, 12500, 1000])], axis=1)
        tbl_0 = 0.05 * jax.random.normal(jax.random.fold_in(_tk, 500 + 0), (1250, 128), jnp.float32)
        tbl_1 = 0.05 * jax.random.normal(jax.random.fold_in(_tk, 500 + 1), (12500, 128), jnp.float32)
        tbl_2 = 0.05 * jax.random.normal(jax.random.fold_in(_tk, 500 + 2), (1000, 128), jnp.float32)
        tbl_3 = 0.05 * jax.random.normal(jax.random.fold_in(_tk, 500 + 3), (1000, 128), jnp.float32)
        tbl_4 = 0.05 * jax.random.normal(jax.random.fold_in(_tk, 500 + 4), (1250, 128), jnp.float32)
        tbl_5 = 0.05 * jax.random.normal(jax.random.fold_in(_tk, 500 + 5), (1250, 128), jnp.float32)
        tbl_6 = 0.05 * jax.random.normal(jax.random.fold_in(_tk, 500 + 6), (1000, 128), jnp.float32)
        tbl_7 = 0.05 * jax.random.normal(jax.random.fold_in(_tk, 500 + 7), (1000, 128), jnp.float32)
        tbl_8 = 0.05 * jax.random.normal(jax.random.fold_in(_tk, 500 + 8), (1000, 128), jnp.float32)
        tbl_9 = 0.05 * jax.random.normal(jax.random.fold_in(_tk, 500 + 9), (125000, 128), jnp.float32)
        tbl_10 = 0.05 * jax.random.normal(jax.random.fold_in(_tk, 500 + 10), (12500, 128), jnp.float32)
        tbl_11 = 0.05 * jax.random.normal(jax.random.fold_in(_tk, 500 + 11), (12500, 128), jnp.float32)
        tbl_12 = 0.05 * jax.random.normal(jax.random.fold_in(_tk, 500 + 12), (1000, 128), jnp.float32)
        tbl_13 = 0.05 * jax.random.normal(jax.random.fold_in(_tk, 500 + 13), (12500, 128), jnp.float32)
        tbl_14 = 0.05 * jax.random.normal(jax.random.fold_in(_tk, 500 + 14), (1250, 128), jnp.float32)
        tbl_15 = 0.05 * jax.random.normal(jax.random.fold_in(_tk, 500 + 15), (12500, 128), jnp.float32)
        tbl_16 = 0.05 * jax.random.normal(jax.random.fold_in(_tk, 500 + 16), (1000, 128), jnp.float32)
        tbl_17 = 0.05 * jax.random.normal(jax.random.fold_in(_tk, 500 + 17), (1250, 128), jnp.float32)
        tbl_18 = 0.05 * jax.random.normal(jax.random.fold_in(_tk, 500 + 18), (1250, 128), jnp.float32)
        tbl_19 = 0.05 * jax.random.normal(jax.random.fold_in(_tk, 500 + 19), (1000, 128), jnp.float32)
        tbl_20 = 0.05 * jax.random.normal(jax.random.fold_in(_tk, 500 + 20), (12500, 128), jnp.float32)
        tbl_21 = 0.05 * jax.random.normal(jax.random.fold_in(_tk, 500 + 21), (1250, 128), jnp.float32)
        tbl_22 = 0.05 * jax.random.normal(jax.random.fold_in(_tk, 500 + 22), (1000, 128), jnp.float32)
        tbl_23 = 0.05 * jax.random.normal(jax.random.fold_in(_tk, 500 + 23), (12500, 128), jnp.float32)
        tbl_24 = 0.05 * jax.random.normal(jax.random.fold_in(_tk, 500 + 24), (1000, 128), jnp.float32)
        tbl_25 = 0.05 * jax.random.normal(jax.random.fold_in(_tk, 500 + 25), (12500, 128), jnp.float32)
        tbl_26 = 0.05 * jax.random.normal(jax.random.fold_in(_tk, 500 + 26), (1000, 128), jnp.float32)
        _rk = jax.random.fold_in(_tk, 7)
        W_top1 = 0.0521996 * jax.random.normal(jax.random.fold_in(_tk, 801), (367, 512), jnp.float32)
        W_top2 = 0.0441942 * jax.random.normal(jax.random.fold_in(_tk, 802), (512, 256), jnp.float32)
        W_top3 = 0.0625 * jax.random.normal(jax.random.fold_in(_tk, 803), (256, 1), jnp.float32)
        b_top1 = jnp.zeros((512,), jnp.float32)
        b_top2 = jnp.zeros((256,), jnp.float32)
        return (dense_ctx, ids, tbl_0, tbl_1, tbl_2, tbl_3, tbl_4, tbl_5, tbl_6, tbl_7, tbl_8, tbl_9, tbl_10, tbl_11, tbl_12, tbl_13, tbl_14, tbl_15, tbl_16, tbl_17, tbl_18, tbl_19, tbl_20, tbl_21, tbl_22, tbl_23, tbl_24, tbl_25, tbl_26, W_top1, b_top1, W_top2, b_top2, W_top3)
    dense_ctx, ids, tbl_0, tbl_1, tbl_2, tbl_3, tbl_4, tbl_5, tbl_6, tbl_7, tbl_8, tbl_9, tbl_10, tbl_11, tbl_12, tbl_13, tbl_14, tbl_15, tbl_16, tbl_17, tbl_18, tbl_19, tbl_20, tbl_21, tbl_22, tbl_23, tbl_24, tbl_25, tbl_26, W_top1, b_top1, W_top2, b_top2, W_top3 = _rec_inputs()

    def _L0_rec_setup():
        import jax, jax.numpy as jnp
        import numpy as np

        def _tri_indices(num_feas):
            return np.array([i * num_feas + j for j in range(1, num_feas) for i in range(j)], dtype=np.int32)
        key = jax.random.key(seed)
        batch, num_feas, embed_dim = (2048, 27, 128)
        inputs = jax.random.normal(key, (batch, num_feas, embed_dim), dtype=jnp.float32)
        return {'inputs': inputs, 'num_feas': num_feas}
    _L0_rec_all = _L0_rec_setup()
    _L0_rec_in = {k: v for k, v in _L0_rec_all.items() if k in ()}
    del _L0_rec_all
    return {'dense_ctx': dense_ctx, 'ids': ids, 'tbl_0': tbl_0, 'tbl_1': tbl_1, 'tbl_2': tbl_2, 'tbl_3': tbl_3, 'tbl_4': tbl_4, 'tbl_5': tbl_5, 'tbl_6': tbl_6, 'tbl_7': tbl_7, 'tbl_8': tbl_8, 'tbl_9': tbl_9, 'tbl_10': tbl_10, 'tbl_11': tbl_11, 'tbl_12': tbl_12, 'tbl_13': tbl_13, 'tbl_14': tbl_14, 'tbl_15': tbl_15, 'tbl_16': tbl_16, 'tbl_17': tbl_17, 'tbl_18': tbl_18, 'tbl_19': tbl_19, 'tbl_20': tbl_20, 'tbl_21': tbl_21, 'tbl_22': tbl_22, 'tbl_23': tbl_23, 'tbl_24': tbl_24, 'tbl_25': tbl_25, 'tbl_26': tbl_26, 'W_top1': W_top1, 'b_top1': b_top1, 'W_top2': W_top2, 'b_top2': b_top2, 'W_top3': W_top3}

def reference(dense_ctx, ids, tbl_0, tbl_1, tbl_2, tbl_3, tbl_4, tbl_5, tbl_6, tbl_7, tbl_8, tbl_9, tbl_10, tbl_11, tbl_12, tbl_13, tbl_14, tbl_15, tbl_16, tbl_17, tbl_18, tbl_19, tbl_20, tbl_21, tbl_22, tbl_23, tbl_24, tbl_25, tbl_26, W_top1, b_top1, W_top2, b_top2, W_top3):
    import jax
    import jax.numpy as jnp

    def _L0_rec_ref(inputs, num_feas):
        import jax, jax.numpy as jnp
        import numpy as np

        def _tri_indices(num_feas):
            return np.array([i * num_feas + j for j in range(1, num_feas) for i in range(j)], dtype=np.int32)
        dot = jnp.einsum('bnd,bmd->bnm', inputs, inputs)
        idx = jnp.asarray(_tri_indices(num_feas))
        flat = dot.reshape(inputs.shape[0], num_feas * num_feas)
        return flat[:, idx]
    e = jnp.stack([tbl_0[ids[:, 0]], tbl_1[ids[:, 1]], tbl_2[ids[:, 2]], tbl_3[ids[:, 3]], tbl_4[ids[:, 4]], tbl_5[ids[:, 5]], tbl_6[ids[:, 6]], tbl_7[ids[:, 7]], tbl_8[ids[:, 8]], tbl_9[ids[:, 9]], tbl_10[ids[:, 10]], tbl_11[ids[:, 11]], tbl_12[ids[:, 12]], tbl_13[ids[:, 13]], tbl_14[ids[:, 14]], tbl_15[ids[:, 15]], tbl_16[ids[:, 16]], tbl_17[ids[:, 17]], tbl_18[ids[:, 18]], tbl_19[ids[:, 19]], tbl_20[ids[:, 20]], tbl_21[ids[:, 21]], tbl_22[ids[:, 22]], tbl_23[ids[:, 23]], tbl_24[ids[:, 24]], tbl_25[ids[:, 25]], tbl_26[ids[:, 26]]], axis=1)
    z = _L0_rec_ref(e, 27)
    z = z.reshape(z.shape[0], -1)
    h = jnp.concatenate([z, dense_ctx], axis=1)
    h = jnp.maximum(h @ W_top1 + b_top1, 0.0)
    h = jnp.maximum(h @ W_top2 + b_top2, 0.0)
    y = h @ W_top3
    return y

_drawn_inputs = setup_inputs


def setup_inputs(seed=0):
    import zlib

    import numpy as np

    out = dict(_drawn_inputs(seed))
    spreads = {'b_top1': (0.0, 0.1), 'b_top2': (0.0, 0.1)}
    factors = {}
    for name, (base, spread) in spreads.items():
        noise = np.random.default_rng([zlib.crc32(name.encode()), seed]).standard_normal(out[name].shape)
        drawn = base * np.exp(spread * noise) if base else spread * noise
        out[name] = jnp.asarray(drawn.astype(out[name].dtype))
    for name, factor in factors.items():
        out[name] = (out[name] * factor).astype(out[name].dtype)
    return out
```

```python
import concourse.bass as bass
from concourse import mybir
from contextlib import ExitStack

P = 128
BATCH, D = 2048, 128
FEATURES = 27
DENSE = 16
SIZES = [1250, 12500, 1000, 1000, 1250, 1250, 1000, 1000, 1000, 125000, 12500, 12500, 1000, 12500, 1250,
         12500, 1000, 1250, 1250, 1000, 12500, 1250, 1000, 12500, 1000, 12500, 1000]
ONEHOT = [2, 3, 6, 7, 8, 12, 16, 19]
GATHERED = [f for f in range(FEATURES) if f not in ONEHOT]
SLOTS = GATHERED + ONEHOT
NG, NO = len(GATHERED), len(ONEHOT)

BLK = 256
BLOCKS = BATCH // BLK
TILES = BLK // P
QUAD = 4
NQ = BLK // QUAD
PAD = P // QUAD
VOCAB = 1000
CHUNKS = 8
VP = VOCAB // CHUNKS
HALF = CHUNKS // 2

GROUPS = [range(a, min(a + 4, NG)) for a in range(0, NG, 4)]
NGR = len(GROUPS)
PAIRS_OH = NO // 2
LEAD_UNITS = PAIRS_OH
BLOCK_UNITS = TILES * NGR + PAIRS_OH

QUADS_BANK = 4
UNIT_BANKS = 2
UNIT_Q = QUADS_BANK * UNIT_BANKS
UNITS = NQ // UNIT_Q
UNITS_TILE = UNITS // TILES
SQ = FEATURES * FEATURES

H1, H2 = 512, 256
M1, M2 = H1 // P, H2 // P
MLP_STEPS = M1 + M2 + 1

STRIDE = FEATURES + 1
KMAX = 13
I_CHUNKS = [(0, 9), (9, 18), (18, 26)]
DENSE_HALF = DENSE // 2
DENSE_AT = 9 * KMAX
FAR_AT = 8 * KMAX
K_ROWS = [DENSE_AT + DENSE_HALF, DENSE_AT + DENSE_HALF, FAR_AT + 13]


def onehot_unit(v):
    return NGR + v if v < 2 else 2 * NGR + v


def tile_unit(q, last):
    return q * (NGR + (0 if last else 2))


def build(nc, ids_gather, ids_onehot, dense, tables, w1, b1, w2, b2, w3, y):
    f32, f32r, i32 = mybir.dt.float32, mybir.dt.float32r, mybir.dt.int32
    ALU = mybir.AluOpType
    ACT = mybir.ActivationFunctionType

    dots_dram = nc.dram_tensor("dots_dram", (BLOCKS, SQ, QUAD, NQ), f32).ap()

    with ExitStack() as ctx:
        def sb(name, shape, dt):
            return ctx.enter_context(nc.sbuf_tensor(name, shape, dt))

        def pb(name, shape):
            return ctx.enter_context(nc.psum_tensor(name, shape, f32))

        def sem(name):
            return ctx.enter_context(nc.semaphore(name))

        tab_hi = sb("tab_hi", [P, NO, CHUNKS, D], f32r)
        tab_lo = sb("tab_lo", [P, NO, CHUNKS, D], f32r)
        emb = sb("emb", [P, 2, BLK, PAD], f32)
        rows = sb("rows", [P, TILES, NG, D], f32)
        idx = sb("idx", [P, 2 * TILES, NG], i32)
        idb = sb("idb", [P, 4, BLK], i32)
        mask = sb("mask", [P, 2, HALF, BLK], f32r)
        dots = sb("dots", [P, 2, FEATURES, NQ], f32)
        zT = sb("zT", [P, 2, 3, BLK], f32)
        w1_sb = sb("w1_sb", [P, 3, H1], f32)
        w2_sb = sb("w2_sb", [P, M1, H2], f32)
        w3_sb = sb("w3_sb", [P, M2], f32)
        b1_sb = sb("b1_sb", [P, M1], f32)
        b2_sb = sb("b2_sb", [P, M2], f32)
        h1 = sb("h1", [P, M1, BLK], f32)
        h2 = sb("h2", [P, M2, BLK], f32)
        y_sb = sb("y_sb", [1, 2, BLK], f32)
        ident = sb("ident", [P, P], f32)
        cmp_i = sb("cmp_i", [P, CHUNKS], i32)
        cmp = sb("cmp", [P, CHUNKS], f32)
        staged = emb[0:VP, 1, :, :].rearrange("p a s -> p (a s)").rearrange(
            "p (f n) -> p f n", f=NO)

        emb_ps = pb("emb_ps", [P, 2, 512])
        dots_ps = pb("dots_ps", [P, 2, UNIT_BANKS, 512])
        mlp_ps = pb("mlp_ps", [P, 2, 512])

        table_in = [sem(f"table_in{f}") for f in range(NO)]
        idx_in = [sem(f"idx_in{k}") for k in range(2 * TILES)]
        idb_in = [sem(f"idb_in{k}") for k in range(4)]
        weights_in = sem("weights_in")
        gathered = [[sem(f"gathered{q}_{g}") for g in range(NGR)] for q in range(TILES)]
        ident_zeroed = sem("ident_zeroed")
        ident_ready = sem("ident_ready")
        cmp_iota = sem("cmp_iota")
        cmp_ready = sem("cmp_ready")
        hi_ready = sem("hi_ready")
        lo_ready = sem("lo_ready")
        pads_zero = sem("pads_zero")
        mask_ready = sem("mask_ready")
        mask_used = sem("mask_used")
        tile_full = sem("tile_full")
        emb_ps_empty = sem("emb_ps_empty")
        dots_ps_full = sem("dots_ps_full")
        dots_ps_empty = sem("dots_ps_empty")
        mlp_ps_full = sem("mlp_ps_full")
        mlp_ps_empty = sem("mlp_ps_empty")
        dots_out = [sem(f"dots_out{k}") for k in range(2)]
        z_in = [sem(f"z_in{k}") for k in range(2)]
        y_out = [sem(f"y_out{k}") for k in range(2)]

        block = ctx.enter_context(nc.Block())

        def unit0(b):
            return LEAD_UNITS + BLOCK_UNITS * b

        def run_blocks(engine, step):
            step(0, 0, 0)
            with engine.Fori(0, BLOCKS // 2 - 1) as pair:
                step(2 * pair + 1, 1, pair)
                step(2 * pair + 2, 0, pair + 1)
            step(BLOCKS - 1, 1, BLOCKS // 2 - 1)

        def is_int(x, v):
            return isinstance(x, int) and x == v

        @block.sync
        def _(sp):
            def load_idx(b, parity, nth):
                for q in range(TILES):
                    k = parity * TILES + q
                    sp.dma_start(idx[:, k, :], ids_gather[:, bass.ds((b * TILES + q) * NG, NG)]
                                 ).then_inc(idx_in[k], 16)

            def load_idb(b, f):
                sp.dma_start(idb[:, f % 4, :],
                             ids_onehot[f:f + 1, bass.ds(b * BLK, BLK)].broadcast_to([P, BLK])
                             ).then_inc(idb_in[f % 4], 16)

            def store_y(b, parity):
                sp.wait_ge(mlp_ps_empty, MLP_STEPS * b + MLP_STEPS)
                sp.dma_start(y[0:1, bass.ds(b * BLK, BLK)], y_sb[0:1, parity, :]).then_inc(y_out[parity], 16)

            load_idx(0, 0, 0)
            for f in range(4):
                load_idb(0, f)
            for f in range(NO):
                for a, z in ((0, 112), (112, VP)):
                    sp.dma_start(staged[a:z, f, :],
                                 tables[ONEHOT[f]].rearrange("(p c) d -> p (c d)", c=CHUNKS)[a:z, :]
                                 ).then_inc(table_in[f], 16)
            row = 0
            for c in range(3):
                sp.dma_start(w1_sb[0:K_ROWS[c], c, :], w1[row:row + K_ROWS[c], :]).then_inc(weights_in, 16)
                row += K_ROWS[c]
            sp.dma_start(w2_sb[:, :, :], w2.rearrange("(m p) n -> p m n", p=P)).then_inc(weights_in, 16)
            sp.dma_start(w3_sb[:, :], w3).then_inc(weights_in, 16)
            sp.dma_start(b1_sb[:, :], b1).then_inc(weights_in, 16)
            sp.dma_start(b2_sb[:, :], b2).then_inc(weights_in, 16)
            for f in range(4, NO):
                sp.wait_ge(mask_ready, 2 * (f - 4) + 2)
                load_idb(0, f)

            def step(b, parity, nth):
                last = is_int(b, BLOCKS - 1)
                if not last:
                    if not is_int(b, 0):
                        sp.wait_ge(tile_full, TILES * NGR * b)
                    load_idx(b + 1, 1 - parity, nth)
                    for f in range(NO):
                        sp.wait_ge(mask_ready, 2 * (NO * (b + 1) + f - 4) + 2)
                        load_idb(b + 1, f)
                if not is_int(b, 0):
                    store_y(b - 1, 1 - parity)
                sp.wait_ge(dots_ps_empty, UNITS * b + UNITS)
                square = dots_dram[bass.ds(b, 1), :, :, :].rearrange(
                    "o (i j) s g -> (o i) j s g", j=FEATURES)
                for s in range(QUAD):
                    sp.dma_start(square[:, :, s, :], dots[PAD * s:PAD * s + FEATURES, parity, :, :]
                                 ).then_inc(dots_out[parity], 16)
                if not is_int(b, 0):
                    sp.wait_ge(mlp_ps_full, MLP_STEPS * (b - 1))
                sp.wait_ge(dots_out[parity], 16 * QUAD * (nth + 1))
                flat = dots_dram[bass.ds(b, 1), 0:STRIDE * 26, :, :].rearrange(
                    "o (i c) s g -> (o i) c (s g)", c=STRIDE)
                for c, (a, z) in enumerate(I_CHUNKS):
                    sp.dma_start(zT[0:(z - a) * KMAX, parity, c, :], flat[a:z, 1:KMAX + 1, :]
                                 ).then_inc(z_in[parity], 16)
                sp.dma_start(zT[FAR_AT:FAR_AT + 13, parity, 2, :], flat[0:13, KMAX + 1, :]
                             ).then_inc(z_in[parity], 16)
                for c in range(2):
                    sp.dma_start(zT[DENSE_AT:DENSE_AT + DENSE_HALF, parity, c, :],
                                 dense[c * DENSE_HALF:(c + 1) * DENSE_HALF, bass.ds(b * BLK, BLK)]
                                 ).then_inc(z_in[parity], 16)

            run_blocks(sp, step)
            store_y(BLOCKS - 1, 1)
            for k in range(2):
                sp.wait_ge(y_out[k], 16 * (BLOCKS // 2))

        @block.gpsimd
        def _(pool):
            nc.gpsimd.iota(cmp_i[:, :], pattern=[[1, CHUNKS]], base=0, channel_multiplier=CHUNKS
                           ).then_inc(cmp_iota, 1)
            nc.gpsimd.memset(ident[:, :], 0.0).then_inc(ident_zeroed, 1)
            pool.wait_ge(ident_zeroed, 1)
            nc.gpsimd.affine_select(out=ident[:, :], in_=ident[:, :], compare_op=ALU.not_equal, fill=1.0,
                                    base=0, pattern=[[-1, P]], channel_multiplier=1).then_inc(ident_ready, 1)

            groups_read = pool.alloc_register("groups_read")
            idx_count = [pool.alloc_register(f"idx_count{k}") for k in range(2)]
            for reg in [groups_read] + idx_count:
                pool.reg_mov(reg, 0)

            def step(b, parity, nth):
                pool.reg_add(idx_count[parity], idx_count[parity], 16)
                for q in range(TILES):
                    k = parity * TILES + q
                    for g, group in enumerate(GROUPS):
                        if not is_int(b, 0):
                            pool.reg_add(groups_read, groups_read, 1)
                        pool.wait_ge(ident_ready, 1)
                        if g == 0:
                            pool.wait_ge(idx_in[k], idx_count[parity])
                        if not is_int(b, 0):
                            pool.wait_ge(tile_full, groups_read)
                        for r in group:
                            nc.gpsimd.indirect_dma_start(
                                rows[:, q, r, :], None, tables[GATHERED[r]][:, :],
                                bass.IndirectOffsetOnAxis(idx[:, k, r:r + 1], 0)).then_inc(gathered[q][g], 16)

            run_blocks(pool, step)

        @block.scalar
        def _(act):
            for f in range(NO):
                act.wait_ge(table_in[f], 32)
                nc.scalar.copy(tab_hi[0:VP, f, :, :], staged[:, f, :].rearrange("p (c d) -> p c d", c=CHUNKS)
                               ).then_inc(hi_ready, 1)

            def empty_onehot(b, offset, v, parity):
                act.wait_ge(mask_used, 2 * (NO * b + 2 * v + 2))
                nc.scalar.copy(emb[:, parity, :, NG + 2 * v:NG + 2 * v + 2],
                               emb_ps[:, offset % 2, :].rearrange("p (k b) -> p b k", k=2)
                               ).then_inc(emb_ps_empty, 1)

            def empty_tile(b, parity, q, last):
                for g, group in enumerate(GROUPS):
                    offset = tile_unit(q, last) + g
                    act.wait_ge(tile_full, TILES * NGR * b + NGR * q + g + 1)
                    k = len(group)
                    nc.scalar.copy(emb[:, parity, q * P:(q + 1) * P, group[0]:group[0] + k],
                                   emb_ps[:, offset % 2, 0:k * P].rearrange("p (k b) -> p b k", k=k)
                                   ).then_inc(emb_ps_empty, 1)

            def relu(b, m):
                act.wait_ge(mlp_ps_full, MLP_STEPS * b + m // 2 * 2 + 2)
                if m < M1:
                    out, bias, at = h1[:, m, :], b1_sb[:, m:m + 1], m
                else:
                    out, bias, at = h2[:, m - M1, :], b2_sb[:, m - M1:m - M1 + 1], m - M1
                nc.scalar.activation(out, mlp_ps[:, at // 2, at % 2 * BLK:(at % 2 + 1) * BLK], ACT.Relu,
                                     bias=bias).then_inc(mlp_ps_empty, 1)

            def empty_y(b, parity):
                act.wait_ge(mlp_ps_full, MLP_STEPS * b + MLP_STEPS)
                nc.scalar.copy(y_sb[0:1, parity, :].rearrange("p (g s) -> p g s", s=QUAD),
                               mlp_ps[0:1, 1, 0:BLK].rearrange("p (s g) -> p g s", s=QUAD)
                               ).then_inc(mlp_ps_empty, 1)

            for v in range(PAIRS_OH):
                empty_onehot(0, v, v, 0)

            act.wait_ge(weights_in, 16 * 7)
            act.wait_ge(pads_zero, 1)

            def step(b, parity, nth):
                first, last = is_int(b, 0), is_int(b, BLOCKS - 1)
                empty_tile(b, parity, 0, last)
                if not last:
                    empty_onehot(b + 1, onehot_unit(0), 0, 1 - parity)
                if not first:
                    for m in range(M1 + M2):
                        relu(b - 1, m)
                if not last:
                    empty_onehot(b + 1, onehot_unit(1), 1, 1 - parity)
                if not first:
                    if parity == 1:
                        act.wait_ge(y_out[0], 16 * nth)
                    else:
                        act.wait_ge(y_out[1], 16 * (nth - 1))
                    empty_y(b - 1, 1 - parity)
                empty_tile(b, parity, 1, last)
                if not last:
                    for v in (2, 3):
                        empty_onehot(b + 1, onehot_unit(v), v, 1 - parity)

            run_blocks(act, step)
            for m in range(M1 + M2):
                relu(BLOCKS - 1, m)
            act.wait_ge(y_out[1], 16 * (BLOCKS // 2 - 1))
            empty_y(BLOCKS - 1, 1)

        @block.vector
        def _(dve):
            nc.vector.memset(emb[:, 0, :, FEATURES:PAD], 0.0)
            dve.wait_ge(cmp_iota, 1)
            nc.vector.tensor_copy(cmp[:, :], cmp_i[:, :]).then_inc(cmp_ready, 1)
            dve.wait_ge(cmp_ready, 1)

            def masks(b, f, ids_before):
                dve.wait_ge(idb_in[f % 4], 16 * (ids_before + 1))
                for h in range(2):
                    n = 2 * (NO * b + f) + h
                    if not (isinstance(n, int) and n < 2):
                        dve.wait_ge(mask_used, n - 1)
                    for c in range(HALF):
                        at = h * HALF + c
                        made = nc.vector.tensor_scalar(mask[0:VP, h, c, :], idb[0:VP, f % 4, :],
                                                       cmp[0:VP, at:at + 1], None, ALU.is_equal)
                    made.then_inc(mask_ready, 1)

            for f in range(NO):
                dve.wait_ge(hi_ready, f + 1)
                nc.vector.tensor_tensor(
                    tab_lo[0:VP, f, :, :].rearrange("p c d -> p (c d)"), staged[:, f, :],
                    tab_hi[0:VP, f, :, :].rearrange("p c d -> p (c d)").bitcast(f32),
                    ALU.subtract).then_inc(lo_ready, 1)
                masks(0, f, f // 4)
            dve.wait_ge(lo_ready, NO)
            nc.vector.memset(emb[:, 1, :, FEATURES:PAD], 0.0).then_inc(pads_zero, 1)

            def step(b, parity, nth):
                last = is_int(b, BLOCKS - 1)
                if not is_int(b, 0):
                    dve.wait_ge(dots_out[parity], 16 * QUAD * nth)
                for u in range(UNITS):
                    if not last:
                        masks(b + 1, u, (b + 1) * (NO // 4) + u // 4)
                    dve.wait_ge(dots_ps_full, UNITS * b + u + 1)
                    for s in range(QUAD):
                        a, z = PAD * s, PAD * s + FEATURES
                        src = dots_ps[a:z, u % 2, :, 0:QUADS_BANK * QUAD * FEATURES].rearrange(
                            "p a (c t j) -> p a c t j", c=QUADS_BANK, t=QUAD)[:, :, :, s, :]
                        dst = dots[a:z, parity, :, u * UNIT_Q:(u + 1) * UNIT_Q].rearrange(
                            "p j (a c) -> p a c j", a=UNIT_BANKS)
                        taken = nc.vector.tensor_copy(dst, src)
                    taken.then_inc(dots_ps_empty, 1)

            run_blocks(dve, step)

        @block.tensor
        def _(pe):
            def onehot(b, f, n, offset):
                if f % 2 == 0 and not (isinstance(n, int) and n < 2):
                    pe.wait_ge(emb_ps_empty, n - 1)
                out = emb_ps[:, offset % 2, f % 2 * BLK:(f % 2 + 1) * BLK]
                for h in range(2):
                    pe.wait_ge(mask_ready, 2 * (NO * b + f) + h + 1)
                    for c in range(HALF):
                        at = h * HALF + c
                        nc.tensor.matmul(out, tab_hi[0:VP, f, at, :], mask[0:VP, h, c, :],
                                         start=(at == 0), stop=False)
                        done = nc.tensor.matmul(out, tab_lo[0:VP, f, at, :], mask[0:VP, h, c, :],
                                                start=False, stop=(at == CHUNKS - 1))
                    done.then_inc(mask_used, 1)

            def tile(b, q, nth, last):
                for g, group in enumerate(GROUPS):
                    offset = tile_unit(q, last) + g
                    pe.wait_ge(emb_ps_empty, unit0(b) + offset - 1)
                    pe.wait_ge(gathered[q][g], 16 * len(group) * (b + 1))
                    for i, r in enumerate(group):
                        done = nc.tensor.transpose(emb_ps[:, offset % 2, i * P:(i + 1) * P], rows[:, q, r, :],
                                                   ident[:, :])
                    done.then_inc(tile_full, 1)

            def dot_unit(b, parity, u):
                n = UNITS * b + u
                if not (isinstance(n, int) and n < 2):
                    pe.wait_ge(dots_ps_empty, n - 1)
                for i in range(UNIT_Q):
                    at = (u * UNIT_Q + i) * QUAD
                    col = i % QUADS_BANK * QUAD * FEATURES
                    done = nc.tensor.matmul(
                        dots_ps[:, u % 2, i // QUADS_BANK, col:col + QUAD * FEATURES].rearrange(
                            "p (t j) -> p t j", t=QUAD),
                        emb[:, parity, at:at + QUAD, :], emb[:, parity, at:at + QUAD, 0:FEATURES],
                        start=True, stop=True)
                done.then_inc(dots_ps_full, 1)

            def layer1(b, parity, nth):
                pe.wait_ge(z_in[parity], 16 * 6 * (nth + 1))
                pe.wait_ge(mlp_ps_empty, MLP_STEPS * b)
                for m in range(M1):
                    for c in range(3):
                        done = nc.tensor.matmul(mlp_ps[:, m // 2, m % 2 * BLK:(m % 2 + 1) * BLK],
                                                w1_sb[0:K_ROWS[c], c, m * P:(m + 1) * P],
                                                zT[0:K_ROWS[c], parity, c, :], start=(c == 0), stop=(c == 2))
                    done.then_inc(mlp_ps_full, 1)

            def layer2(b):
                pe.wait_ge(mlp_ps_empty, MLP_STEPS * b + M1)
                for m in range(M2):
                    for c in range(M1):
                        done = nc.tensor.matmul(mlp_ps[:, 0, m * BLK:(m + 1) * BLK],
                                                w2_sb[:, c, m * P:(m + 1) * P], h1[:, c, :],
                                                start=(c == 0), stop=(c == M1 - 1))
                    done.then_inc(mlp_ps_full, 1)

            def layer3(b):
                pe.wait_ge(mlp_ps_empty, MLP_STEPS * b + M1 + M2)
                for c in range(M2):
                    done = nc.tensor.matmul(mlp_ps[0:1, 1, 0:BLK], w3_sb[:, c:c + 1], h2[:, c, :],
                                            start=(c == 0), stop=(c == M2 - 1))
                done.then_inc(mlp_ps_full, 1)

            for f in range(NO):
                pe.wait_ge(lo_ready, f + 1)
                onehot(0, f, f // 2, f // 2)
            pe.wait_ge(ident_ready, 1)
            pe.wait_ge(weights_in, 16 * 7)
            pe.wait_ge(pads_zero, 1)

            def step(b, parity, nth):
                first, last = is_int(b, 0), is_int(b, BLOCKS - 1)
                for q in range(TILES):
                    tile(b, q, nth, last)
                    pe.wait_ge(emb_ps_empty, unit0(b) + tile_unit(q, last) + NGR)
                    for i in range(UNITS_TILE):
                        u = q * UNITS_TILE + i
                        dot_unit(b, parity, u)
                        if not last:
                            v = u // 2
                            onehot(b + 1, u, unit0(b) + onehot_unit(v), onehot_unit(v))
                        if not first and q == 0:
                            if i == 1:
                                layer1(b - 1, 1 - parity, nth - (1 if parity == 0 else 0))
                            if i == 2:
                                layer2(b - 1)
                            if i == 3:
                                layer3(b - 1)

            run_blocks(pe, step)
            layer1(BLOCKS - 1, 1, BLOCKS // 2 - 1)
            layer2(BLOCKS - 1)
            layer3(BLOCKS - 1)


def pair_column(a, c):
    i, j = min(a, c), max(a, c)
    return j * (j - 1) // 2 + i


def layer1_rows():
    pairs = FEATURES * (FEATURES - 1) // 2

    def pair(row):
        return pair_column(SLOTS[row // FEATURES], SLOTS[row % FEATURES])

    order = []
    for c, (a, z) in enumerate(I_CHUNKS):
        order += [pair(STRIDE * i + k) for i in range(a, z) for k in range(1, KMAX + 1)]
        if c < 2:
            order += [pairs + c * DENSE_HALF + i for i in range(DENSE_HALF)]
    order += [pair(STRIDE * i + KMAX + 1) for i in range(13)]
    return order


def kernel(**inputs):
    import numpy as _np
    import concourse.bacc as _bacc
    from concourse import mybir as _mybir
    from concourse.bass_utils import run_bass_kernel_spmd as _run

    nc = _bacc.Bacc("TRN2", target_bir_lowering=False, num_devices=1)
    ids = _np.asarray(inputs["ids"])
    arrays = {
        "ids_gather": ids.reshape(BATCH // P, P, FEATURES)[:, :, GATHERED].transpose(1, 0, 2).reshape(P, -1),
        "ids_onehot": ids[:, ONEHOT].T,
        "dense": _np.asarray(inputs["dense_ctx"]).reshape(BLOCKS, NQ, QUAD, DENSE).transpose(
            3, 0, 2, 1).reshape(DENSE, BATCH),
        "w1": _np.asarray(inputs["W_top1"])[layer1_rows(), :],
        "b1": _np.asarray(inputs["b_top1"]).reshape(M1, P).T,
        "w2": _np.asarray(inputs["W_top2"]),
        "b2": _np.asarray(inputs["b_top2"]).reshape(M2, P).T,
        "w3": _np.asarray(inputs["W_top3"]).reshape(M2, P).T,
    }
    for f in range(FEATURES):
        arrays[f"tbl_{f}"] = _np.asarray(inputs[f"tbl_{f}"])
    arrays = {k: _np.ascontiguousarray(v) for k, v in arrays.items()}
    aps = {k: nc.dram_tensor(k, v.shape, _mybir.dt.from_np(v.dtype), kind="ExternalInput").ap()
           for k, v in arrays.items()}
    y = nc.dram_tensor("y", (1, BATCH), _mybir.dt.float32, kind="ExternalOutput").ap()
    build(nc, aps["ids_gather"], aps["ids_onehot"], aps["dense"], [aps[f"tbl_{f}"] for f in range(FEATURES)],
          aps["w1"], aps["b1"], aps["w2"], aps["b2"], aps["w3"], y)
    r = _run(nc, [arrays], core_ids=[0])
    return r.results[0]["y"].reshape(BATCH, 1)
```

```python
import concourse.bass as bass
from concourse import mybir
from contextlib import ExitStack

P = 128
BATCH, D = 2048, 128
FEATURES = 27
DENSE = 16
SIZES = [1250, 12500, 1000, 1000, 1250, 1250, 1000, 1000, 1000, 125000, 12500, 12500, 1000, 12500, 1250,
         12500, 1000, 1250, 1250, 1000, 12500, 1250, 1000, 12500, 1000, 12500, 1000]
ONEHOT = [2, 3, 6, 7, 8, 12, 16, 19]
GATHERED = [f for f in range(FEATURES) if f not in ONEHOT]
SLOTS = GATHERED + ONEHOT
NG, NO = len(GATHERED), len(ONEHOT)

BLK = 256
BLOCKS = BATCH // BLK
TILES = BLK // P
QUAD = 4
NQ = BLK // QUAD
PAD = P // QUAD
VOCAB = 1000
CHUNKS = 8
VP = VOCAB // CHUNKS
HALF = CHUNKS // 2

GROUPS = [range(a, min(a + 4, NG)) for a in range(0, NG, 4)]
NGR = len(GROUPS)
PAIRS_OH = NO // 2

QUADS_BANK = 4
UNIT_BANKS = 2
UNIT_Q = QUADS_BANK * UNIT_BANKS
UNITS = NQ // UNIT_Q
UNITS_TILE = UNITS // TILES
SQ = FEATURES * FEATURES

H1, H2 = 512, 256
M1, M2 = H1 // P, H2 // P
MLP_STEPS = M1 + M2 + 1

STRIDE = FEATURES + 1
KMAX = 13
I_CHUNKS = [(0, 9), (9, 18), (18, 26)]
DENSE_HALF = DENSE // 2
DENSE_AT = 9 * KMAX
FAR_AT = 8 * KMAX
K_ROWS = [DENSE_AT + DENSE_HALF, DENSE_AT + DENSE_HALF, FAR_AT + 13]


assert NGR == UNITS_TILE + 1


def build(nc, ids_gather, ids_onehot, dense, tables, w1, b1, w2, b2, w3, y):
    f32, f32r, i32 = mybir.dt.float32, mybir.dt.float32r, mybir.dt.int32
    ALU = mybir.AluOpType
    ACT = mybir.ActivationFunctionType

    dots_dram = nc.dram_tensor("dots_dram", (BLOCKS, SQ, QUAD, NQ), f32).ap()

    with ExitStack() as ctx:
        def sb(name, shape, dt):
            return ctx.enter_context(nc.sbuf_tensor(name, shape, dt))

        def pb(name, shape):
            return ctx.enter_context(nc.psum_tensor(name, shape, f32))

        def sem(name):
            return ctx.enter_context(nc.semaphore(name))

        tab_hi = sb("tab_hi", [P, NO, CHUNKS, D], f32r)
        tab_lo = sb("tab_lo", [P, NO, CHUNKS, D], f32r)
        emb = sb("emb", [P, 2, BLK, PAD], f32)
        rows = sb("rows", [P, TILES, NG, D], f32)
        idx = sb("idx", [P, 2 * TILES, NG], i32)
        idb = sb("idb", [P, 4, BLK], i32)
        mask = sb("mask", [P, 2, HALF, BLK], f32r)
        dots = sb("dots", [P, 2, FEATURES, NQ], f32)
        zT = sb("zT", [P, 2, 3, BLK], f32)
        w1_sb = sb("w1_sb", [P, 3, H1], f32)
        w2_sb = sb("w2_sb", [P, M1, H2], f32)
        w3_sb = sb("w3_sb", [P, M2], f32)
        b1_sb = sb("b1_sb", [P, M1], f32)
        b2_sb = sb("b2_sb", [P, M2], f32)
        h1 = sb("h1", [P, M1, BLK], f32)
        h2 = sb("h2", [P, M2, BLK], f32)
        y_sb = sb("y_sb", [1, 2, BLK], f32)
        ident = sb("ident", [P, P], f32)
        cmp_i = sb("cmp_i", [P, CHUNKS], i32)
        cmp = sb("cmp", [P, CHUNKS], f32)
        staged = emb[0:VP, 1, :, :].rearrange("p a s -> p (a s)").rearrange(
            "p (f n) -> p f n", f=NO)

        tile_ps = pb("tile_ps", [P, 512])
        onehot_ps = pb("onehot_ps", [P, 512])
        dots_ps = pb("dots_ps", [P, 2, UNIT_BANKS, 512])
        mlp_ps = pb("mlp_ps", [P, 2, 512])

        table_in = [sem(f"table_in{f}") for f in range(NO)]
        idx_in = [sem(f"idx_in{k}") for k in range(2 * TILES)]
        idb_in = [sem(f"idb_in{k}") for k in range(4)]
        weights_in = sem("weights_in")
        gathered = [[sem(f"gathered{q}_{g}") for g in range(NGR)] for q in range(TILES)]
        ident_zeroed = sem("ident_zeroed")
        ident_ready = sem("ident_ready")
        cmp_iota = sem("cmp_iota")
        cmp_ready = sem("cmp_ready")
        hi_ready = sem("hi_ready")
        lo_ready = sem("lo_ready")
        pads_zero = sem("pads_zero")
        mask_ready = sem("mask_ready")
        mask_used = sem("mask_used")
        tile_ps_full = sem("tile_ps_full")
        tile_ps_empty = sem("tile_ps_empty")
        onehot_ps_empty = sem("onehot_ps_empty")
        dots_ps_full = sem("dots_ps_full")
        dots_ps_empty_v = sem("dots_ps_empty_v")
        dots_ps_empty_s = sem("dots_ps_empty_s")
        mlp_ps_full = sem("mlp_ps_full")
        mlp_ps_empty = sem("mlp_ps_empty")
        dots_out = [sem(f"dots_out{k}") for k in range(2)]
        z_in = [sem(f"z_in{k}") for k in range(2)]
        MLP_CREDIT, DOTS_CREDIT, Y_CREDIT = MLP_STEPS, 1, 2
        dots_stored = sem("dots_stored")
        y_stored = sem("y_stored")
        y_out = [sem(f"y_out{k}") for k in range(2)]

        block = ctx.enter_context(nc.Block())

        def run_blocks(engine, step):
            step(0, 0, 0)
            with engine.Fori(0, BLOCKS // 2 - 1) as pair:
                step(2 * pair + 1, 1, pair)
                step(2 * pair + 2, 0, pair + 1)
            step(BLOCKS - 1, 1, BLOCKS // 2 - 1)

        def empty_dots(copy, engine, b, parity, u, samples, empty):
            engine.wait_ge(dots_ps_full, UNITS * b + u + 1)
            for s in samples:
                a, z = PAD * s, PAD * s + FEATURES
                src = dots_ps[a:z, u % 2, :, 0:QUADS_BANK * QUAD * FEATURES].rearrange(
                    "p a (c t j) -> p a c t j", c=QUADS_BANK, t=QUAD)[:, :, :, s, :]
                dst = dots[a:z, parity, :, u * UNIT_Q:(u + 1) * UNIT_Q].rearrange(
                    "p j (a c) -> p a c j", a=UNIT_BANKS)
                taken = copy(dst, src)
            taken.then_inc(empty, 1)

        def is_int(x, v):
            return isinstance(x, int) and x == v

        @block.sync
        def _(sp):
            sp.sem_inc(dots_stored, DOTS_CREDIT)
            sp.sem_inc(y_stored, Y_CREDIT)

            def load_idx(b, parity, nth):
                for q in range(TILES):
                    k = parity * TILES + q
                    sp.dma_start(idx[:, k, :], ids_gather[:, bass.ds((b * TILES + q) * NG, NG)]
                                 ).then_inc(idx_in[k], 16)

            def load_idb(b, f):
                sp.dma_start(idb[:, f % 4, :],
                             ids_onehot[f:f + 1, bass.ds(b * BLK, BLK)].broadcast_to([P, BLK])
                             ).then_inc(idb_in[f % 4], 16)

            def store_y(b, parity):
                sp.wait_ge(mlp_ps_empty, MLP_CREDIT + MLP_STEPS * (b + 1))
                sp.dma_start(y[0:1, bass.ds(b * BLK, BLK)], y_sb[0:1, parity, :]).then_inc(y_out[parity], 16)

            load_idx(0, 0, 0)
            for f in range(4):
                load_idb(0, f)
            for f in range(NO):
                for a, z in ((0, 112), (112, VP)):
                    sp.dma_start(staged[a:z, f, :],
                                 tables[ONEHOT[f]].rearrange("(p c) d -> p (c d)", c=CHUNKS)[a:z, :]
                                 ).then_inc(table_in[f], 16)
            row = 0
            for c in range(3):
                sp.dma_start(w1_sb[0:K_ROWS[c], c, :], w1[row:row + K_ROWS[c], :]).then_inc(weights_in, 16)
                row += K_ROWS[c]
            sp.dma_start(w2_sb[:, :, :], w2.rearrange("(m p) n -> p m n", p=P)).then_inc(weights_in, 16)
            sp.dma_start(w3_sb[:, :], w3).then_inc(weights_in, 16)
            sp.dma_start(b1_sb[:, :], b1).then_inc(weights_in, 16)
            sp.dma_start(b2_sb[:, :], b2).then_inc(weights_in, 16)
            for f in range(4, NO + 4):
                sp.wait_ge(mask_ready, 2 * (f - 4) + 2)
                load_idb(f // NO, f % NO)

            def step(b, parity, nth):
                last = is_int(b, BLOCKS - 1)
                if not last:
                    if not is_int(b, 0):
                        sp.wait_ge(tile_ps_full, TILES * NGR * b)
                    load_idx(b + 1, 1 - parity, nth)
                    for f in range(4, NO + 4):
                        sp.wait_ge(mask_ready, 2 * (NO * (b + 1) + f - 4) + 2)
                        load_idb(b + 1 + f // NO, f % NO)
                if not is_int(b, 0):
                    store_y(b - 1, 1 - parity)
                sp.wait_ge(dots_ps_empty_v, UNITS * b + UNITS)
                sp.wait_ge(dots_ps_empty_s, UNITS * b + UNITS)
                square = dots_dram[bass.ds(b, 1), :, :, :].rearrange(
                    "o (i j) s g -> (o i) j s g", j=FEATURES)
                for s in range(QUAD):
                    sp.dma_start(square[:, :, s, :], dots[PAD * s:PAD * s + FEATURES, parity, :, :]
                                 ).then_inc(dots_out[parity], 16)
                if not is_int(b, 0):
                    sp.wait_ge(mlp_ps_empty, MLP_STEPS * b)
                sp.wait_ge(dots_out[parity], 16 * QUAD * (nth + 1))
                sp.sem_inc(dots_stored, 1)
                if not is_int(b, 0):
                    sp.wait_ge(y_out[1 - parity], 16 * (nth + (1 if parity == 1 else 0)))
                    sp.sem_inc(y_stored, 1)
                flat = dots_dram[bass.ds(b, 1), 0:STRIDE * 26, :, :].rearrange(
                    "o (i c) s g -> (o i) c (s g)", c=STRIDE)
                for c, (a, z) in enumerate(I_CHUNKS):
                    sp.dma_start(zT[0:(z - a) * KMAX, parity, c, :], flat[a:z, 1:KMAX + 1, :]
                                 ).then_inc(z_in[parity], 16)
                sp.dma_start(zT[FAR_AT:FAR_AT + 13, parity, 2, :], flat[0:13, KMAX + 1, :]
                             ).then_inc(z_in[parity], 16)
                for c in range(2):
                    sp.dma_start(zT[DENSE_AT:DENSE_AT + DENSE_HALF, parity, c, :],
                                 dense[c * DENSE_HALF:(c + 1) * DENSE_HALF, bass.ds(b * BLK, BLK)]
                                 ).then_inc(z_in[parity], 16)

            run_blocks(sp, step)
            store_y(BLOCKS - 1, 1)
            for k in range(2):
                sp.wait_ge(y_out[k], 16 * (BLOCKS // 2))
            for k in range(4):
                sp.wait_ge(idb_in[k], 16 * (2 * BLOCKS + 1))

        @block.gpsimd
        def _(pool):
            nc.gpsimd.iota(cmp_i[:, :], pattern=[[1, CHUNKS]], base=0, channel_multiplier=CHUNKS
                           ).then_inc(cmp_iota, 1)
            nc.gpsimd.memset(ident[:, :], 0.0).then_inc(ident_zeroed, 1)
            pool.wait_ge(ident_zeroed, 1)
            nc.gpsimd.affine_select(out=ident[:, :], in_=ident[:, :], compare_op=ALU.not_equal, fill=1.0,
                                    base=0, pattern=[[-1, P]], channel_multiplier=1).then_inc(ident_ready, 1)

            groups_read = pool.alloc_register("groups_read")
            idx_count = [pool.alloc_register(f"idx_count{k}") for k in range(2)]
            pool.reg_mov(groups_read, 1)
            for reg in idx_count:
                pool.reg_mov(reg, 16)

            def step(b, parity, nth):
                for q in range(TILES):
                    k = parity * TILES + q
                    for g, group in enumerate(GROUPS):
                        pool.wait_ge(ident_ready, 1)
                        if g == 0:
                            pool.wait_ge(idx_in[k], idx_count[parity])
                        if not is_int(b, 0):
                            pool.wait_ge(tile_ps_full, groups_read)
                            pool.reg_add(groups_read, groups_read, 1)
                        for r in group:
                            nc.gpsimd.indirect_dma_start(
                                rows[:, q, r, :], None, tables[GATHERED[r]][:, :],
                                bass.IndirectOffsetOnAxis(idx[:, k, r:r + 1], 0)).then_inc(gathered[q][g], 16)
                pool.reg_add(idx_count[parity], idx_count[parity], 16)

            run_blocks(pool, step)

        @block.scalar
        def _(act):
            act.sem_inc(mlp_ps_empty, MLP_CREDIT)
            for f in range(NO):
                act.wait_ge(table_in[f], 32)
                nc.scalar.copy(tab_hi[0:VP, f, :, :], staged[:, f, :].rearrange("p (c d) -> p c d", c=CHUNKS)
                               ).then_inc(hi_ready, 1)

            def empty_onehot(b, parity, v):
                act.wait_ge(mask_used, 2 * (NO * b + 2 * v + 2))
                nc.scalar.copy(emb[:, parity, :, NG + 2 * v:NG + 2 * v + 2],
                               onehot_ps[:, :].rearrange("p (k b) -> p b k", k=2)).then_inc(onehot_ps_empty, 1)

            def empty_group(b, parity, q, g):
                act.wait_ge(tile_ps_full, NGR * (TILES * b + q) + g + 1)
                k = len(GROUPS[g])
                nc.scalar.copy(emb[:, parity, q * P:(q + 1) * P, GROUPS[g][0]:GROUPS[g][0] + k],
                               tile_ps[:, 0:k * P].rearrange("p (k b) -> p b k", k=k)
                               ).then_inc(tile_ps_empty, 1)

            def relu(b, m):
                act.wait_ge(mlp_ps_full, MLP_STEPS * b + m // 2 * 2 + 2)
                if m < M1:
                    out, bias, at = h1[:, m, :], b1_sb[:, m:m + 1], m
                else:
                    out, bias, at = h2[:, m - M1, :], b2_sb[:, m - M1:m - M1 + 1], m - M1
                nc.scalar.activation(out, mlp_ps[:, at // 2, at % 2 * BLK:(at % 2 + 1) * BLK], ACT.Relu,
                                     bias=bias).then_inc(mlp_ps_empty, 1)

            def empty_y(b, parity):
                act.wait_ge(mlp_ps_full, MLP_STEPS * b + MLP_STEPS)
                nc.scalar.copy(y_sb[0:1, parity, :].rearrange("p (g s) -> p g s", s=QUAD),
                               mlp_ps[0:1, 1, 0:BLK].rearrange("p (s g) -> p g s", s=QUAD)
                               ).then_inc(mlp_ps_empty, 1)

            for v in range(PAIRS_OH):
                empty_onehot(0, 0, v)
            for g in range(NGR):
                empty_group(0, 0, 0, g)

            act.wait_ge(weights_in, 16 * 7)
            act.wait_ge(pads_zero, 1)

            def step(b, parity, nth):
                first, last = is_int(b, 0), is_int(b, BLOCKS - 1)
                act.wait_ge(dots_stored, b)
                for u in range(UNITS):
                    q, i = u // UNITS_TILE, u % UNITS_TILE
                    empty_dots(nc.scalar.copy, act, b, parity, u, (2, 3), dots_ps_empty_s)
                    if q == 0:
                        empty_group(b, parity, 1, i)
                    elif not last:
                        empty_group(b + 1, 1 - parity, 0, i)
                    if not last and u % 2 == 1:
                        empty_onehot(b + 1, 1 - parity, u // 2)
                    if i == UNITS_TILE - 1:
                        if q == 0:
                            empty_group(b, parity, 1, NGR - 1)
                        elif not last:
                            empty_group(b + 1, 1 - parity, 0, NGR - 1)
                    if not first:
                        if u == 3:
                            for m in range(M1):
                                relu(b - 1, m)
                        if u == 4:
                            for m in range(M1, M1 + M2):
                                relu(b - 1, m)
                        if u == 5:
                            act.wait_ge(y_stored, b)
                            empty_y(b - 1, 1 - parity)

            run_blocks(act, step)
            for m in range(M1 + M2):
                relu(BLOCKS - 1, m)
            act.wait_ge(y_stored, BLOCKS)
            empty_y(BLOCKS - 1, 1)

        @block.vector
        def _(dve):
            nc.vector.memset(emb[:, 0, :, FEATURES:PAD], 0.0)
            dve.wait_ge(cmp_iota, 1)
            nc.vector.tensor_copy(cmp[:, :], cmp_i[:, :]).then_inc(cmp_ready, 1)
            dve.wait_ge(cmp_ready, 1)

            def masks(b, f, ids_before):
                dve.wait_ge(idb_in[f % 4], 16 * (ids_before + 1))
                for h in range(2):
                    n = 2 * (NO * b + f) + h
                    if not (isinstance(n, int) and n < 2):
                        dve.wait_ge(mask_used, n - 1)
                    for c in range(HALF):
                        at = h * HALF + c
                        made = nc.vector.tensor_scalar(mask[0:VP, h, c, :], idb[0:VP, f % 4, :],
                                                       cmp[0:VP, at:at + 1], None, ALU.is_equal)
                    made.then_inc(mask_ready, 1)

            for f in range(NO):
                dve.wait_ge(hi_ready, f + 1)
                nc.vector.tensor_tensor(
                    tab_lo[0:VP, f, :, :].rearrange("p c d -> p (c d)"), staged[:, f, :],
                    tab_hi[0:VP, f, :, :].rearrange("p c d -> p (c d)").bitcast(f32),
                    ALU.subtract).then_inc(lo_ready, 1)
                masks(0, f, f // 4)
            dve.wait_ge(lo_ready, NO)
            nc.vector.memset(emb[:, 1, :, FEATURES:PAD], 0.0).then_inc(pads_zero, 1)

            def step(b, parity, nth):
                last = is_int(b, BLOCKS - 1)
                dve.wait_ge(dots_stored, b)
                for u in range(UNITS):
                    if not last:
                        masks(b + 1, u, (b + 1) * (NO // 4) + u // 4)
                    empty_dots(nc.vector.tensor_copy, dve, b, parity, u, (0, 1), dots_ps_empty_v)

            run_blocks(dve, step)

        @block.tensor
        def _(pe):
            def onehot(b, f):
                if f % 2 == 0 and not (is_int(b, 0) and f == 0):
                    pe.wait_ge(onehot_ps_empty, PAIRS_OH * b + f // 2)
                out = onehot_ps[:, f % 2 * BLK:(f % 2 + 1) * BLK]
                for h in range(2):
                    pe.wait_ge(mask_ready, 2 * (NO * b + f) + h + 1)
                    for c in range(HALF):
                        at = h * HALF + c
                        nc.tensor.matmul(out, tab_hi[0:VP, f, at, :], mask[0:VP, h, c, :],
                                         start=(at == 0), stop=False)
                        done = nc.tensor.matmul(out, tab_lo[0:VP, f, at, :], mask[0:VP, h, c, :],
                                                start=False, stop=(at == CHUNKS - 1))
                    done.then_inc(mask_used, 1)

            def tile_group(b, q, g):
                n = NGR * (TILES * b + q) + g
                if not is_int(n, 0):
                    pe.wait_ge(tile_ps_empty, n)
                pe.wait_ge(gathered[q][g], 16 * len(GROUPS[g]) * (b + 1))
                for i, r in enumerate(GROUPS[g]):
                    done = nc.tensor.transpose(tile_ps[:, i * P:(i + 1) * P], rows[:, q, r, :], ident[:, :])
                done.then_inc(tile_ps_full, 1)

            def dot_unit(b, parity, u):
                n = UNITS * b + u
                if not (isinstance(n, int) and n < 2):
                    pe.wait_ge(dots_ps_empty_v, n - 1)
                    pe.wait_ge(dots_ps_empty_s, n - 1)
                for i in range(UNIT_Q):
                    at = (u * UNIT_Q + i) * QUAD
                    col = i % QUADS_BANK * QUAD * FEATURES
                    done = nc.tensor.matmul(
                        dots_ps[:, u % 2, i // QUADS_BANK, col:col + QUAD * FEATURES].rearrange(
                            "p (t j) -> p t j", t=QUAD),
                        emb[:, parity, at:at + QUAD, :], emb[:, parity, at:at + QUAD, 0:FEATURES],
                        start=True, stop=True)
                done.then_inc(dots_ps_full, 1)

            def layer1(b, parity, nth):
                pe.wait_ge(z_in[parity], 16 * 6 * (nth + 1))
                pe.wait_ge(mlp_ps_empty, MLP_CREDIT + MLP_STEPS * b)
                for m in range(M1):
                    for c in range(3):
                        done = nc.tensor.matmul(mlp_ps[:, m // 2, m % 2 * BLK:(m % 2 + 1) * BLK],
                                                w1_sb[0:K_ROWS[c], c, m * P:(m + 1) * P],
                                                zT[0:K_ROWS[c], parity, c, :], start=(c == 0), stop=(c == 2))
                    done.then_inc(mlp_ps_full, 1)

            def layer2(b):
                pe.wait_ge(mlp_ps_empty, MLP_CREDIT + MLP_STEPS * b + M1)
                for m in range(M2):
                    for c in range(M1):
                        done = nc.tensor.matmul(mlp_ps[:, 0, m * BLK:(m + 1) * BLK],
                                                w2_sb[:, c, m * P:(m + 1) * P], h1[:, c, :],
                                                start=(c == 0), stop=(c == M1 - 1))
                    done.then_inc(mlp_ps_full, 1)

            def layer3(b):
                pe.wait_ge(mlp_ps_empty, MLP_CREDIT + MLP_STEPS * b + M1 + M2)
                for c in range(M2):
                    done = nc.tensor.matmul(mlp_ps[0:1, 1, 0:BLK], w3_sb[:, c:c + 1], h2[:, c, :],
                                            start=(c == 0), stop=(c == M2 - 1))
                done.then_inc(mlp_ps_full, 1)

            for f in range(NO):
                pe.wait_ge(lo_ready, f + 1)
                onehot(0, f)
            pe.wait_ge(ident_ready, 1)
            for g in range(NGR):
                tile_group(0, 0, g)
            pe.wait_ge(weights_in, 16 * 7)
            pe.wait_ge(pads_zero, 1)

            def step(b, parity, nth):
                first, last = is_int(b, 0), is_int(b, BLOCKS - 1)

                def next_tile_group(q, g):
                    if q == 0:
                        tile_group(b, 1, g)
                    elif not last:
                        tile_group(b + 1, 0, g)

                for u in range(UNITS):
                    q, i = u // UNITS_TILE, u % UNITS_TILE
                    if i == 0:
                        pe.wait_ge(tile_ps_empty, NGR * (TILES * b + q + 1))
                        pe.wait_ge(onehot_ps_empty, PAIRS_OH * (b + 1))
                    dot_unit(b, parity, u)
                    next_tile_group(q, i)
                    if not last:
                        onehot(b + 1, u)
                    if i == UNITS_TILE - 1:
                        next_tile_group(q, NGR - 1)
                    if not first:
                        if u == 3:
                            layer1(b - 1, 1 - parity, nth - (1 if parity == 0 else 0))
                        if u == 4:
                            layer2(b - 1)
                        if u == 5:
                            layer3(b - 1)

            run_blocks(pe, step)
            layer1(BLOCKS - 1, 1, BLOCKS // 2 - 1)
            layer2(BLOCKS - 1)
            layer3(BLOCKS - 1)


def pair_column(a, c):
    i, j = min(a, c), max(a, c)
    return j * (j - 1) // 2 + i


def layer1_rows():
    pairs = FEATURES * (FEATURES - 1) // 2

    def pair(row):
        return pair_column(SLOTS[row // FEATURES], SLOTS[row % FEATURES])

    order = []
    for c, (a, z) in enumerate(I_CHUNKS):
        order += [pair(STRIDE * i + k) for i in range(a, z) for k in range(1, KMAX + 1)]
        if c < 2:
            order += [pairs + c * DENSE_HALF + i for i in range(DENSE_HALF)]
    order += [pair(STRIDE * i + KMAX + 1) for i in range(13)]
    return order


def kernel(**inputs):
    import numpy as _np
    import concourse.bacc as _bacc
    from concourse import mybir as _mybir
    from concourse.bass_utils import run_bass_kernel_spmd as _run

    nc = _bacc.Bacc("TRN2", target_bir_lowering=False, num_devices=1)
    ids = _np.asarray(inputs["ids"])
    arrays = {
        "ids_gather": ids.reshape(BATCH // P, P, FEATURES)[:, :, GATHERED].transpose(1, 0, 2).reshape(P, -1),
        "ids_onehot": _np.concatenate([ids[:, ONEHOT].T, ids[:BLK, ONEHOT].T], axis=1),
        "dense": _np.asarray(inputs["dense_ctx"]).reshape(BLOCKS, NQ, QUAD, DENSE).transpose(
            3, 0, 2, 1).reshape(DENSE, BATCH),
        "w1": _np.asarray(inputs["W_top1"])[layer1_rows(), :],
        "b1": _np.asarray(inputs["b_top1"]).reshape(M1, P).T,
        "w2": _np.asarray(inputs["W_top2"]),
        "b2": _np.asarray(inputs["b_top2"]).reshape(M2, P).T,
        "w3": _np.asarray(inputs["W_top3"]).reshape(M2, P).T,
    }
    for f in range(FEATURES):
        arrays[f"tbl_{f}"] = _np.asarray(inputs[f"tbl_{f}"])
    arrays = {k: _np.ascontiguousarray(v) for k, v in arrays.items()}
    aps = {k: nc.dram_tensor(k, v.shape, _mybir.dt.from_np(v.dtype), kind="ExternalInput").ap()
           for k, v in arrays.items()}
    y = nc.dram_tensor("y", (1, BATCH), _mybir.dt.float32, kind="ExternalOutput").ap()
    build(nc, aps["ids_gather"], aps["ids_onehot"], aps["dense"], [aps[f"tbl_{f}"] for f in range(FEATURES)],
          aps["w1"], aps["b1"], aps["w2"], aps["b2"], aps["w3"], y)
    r = _run(nc, [arrays], core_ids=[0])
    return r.results[0]["y"].reshape(BATCH, 1)
```

```python
import concourse.bass as bass
from concourse import mybir
from contextlib import ExitStack

P = 128
BATCH, D = 2048, 128
FEATURES = 27
DENSE = 16
SIZES = [1250, 12500, 1000, 1000, 1250, 1250, 1000, 1000, 1000, 125000, 12500, 12500, 1000, 12500, 1250,
         12500, 1000, 1250, 1250, 1000, 12500, 1250, 1000, 12500, 1000, 12500, 1000]
ONEHOT = [2, 3, 6, 7, 8, 12, 16, 19]
GATHERED = [f for f in range(FEATURES) if f not in ONEHOT]
SLOTS = GATHERED + ONEHOT
NG, NO = len(GATHERED), len(ONEHOT)

DMA_RING = 6144

BLK = 256
BLOCKS = BATCH // BLK
TILES = BLK // P
QUAD = 4
NQ = BLK // QUAD
PAD = P // QUAD
VOCAB = 1000
CHUNKS = 8
VP = VOCAB // CHUNKS
HALF = CHUNKS // 2

GROUPS = [range(a, min(a + 4, NG)) for a in range(0, NG, 4)]
NGR = len(GROUPS)
IDB_LOADS = [range(0, 4), range(4, NO)]
PAIRS_OH = [range(a, min(a + 2, NO)) for a in range(0, NO, 2)]
NPO = len(PAIRS_OH)

QUADS_BANK = 4
UNIT_BANKS = 2
UNIT_Q = QUADS_BANK * UNIT_BANKS
UNITS = NQ // UNIT_Q
UNITS_TILE = UNITS // TILES
SQ = PAD * FEATURES

H1, H2 = 512, 256
M1, M2 = H1 // P, H2 // P
MLP_STEPS = M1 + M2 + 1

STRIDE = FEATURES + 1
KMAX = 13
I_CHUNKS = [(0, 9), (9, 18), (18, 26)]
DENSE_HALF = DENSE // 2
DENSE_AT = 9 * KMAX
FAR_AT = 8 * KMAX
BIAS_AT = FAR_AT + 13
K_ROWS = [DENSE_AT + DENSE_HALF, DENSE_AT + DENSE_HALF, BIAS_AT + 1]

GROUPS_AT = [([0], []), ([1], []), ([2], []), ([3], [4])]
assert len(GROUPS_AT) == UNITS_TILE and sum(len(a) + len(z) for a, z in GROUPS_AT) == NGR

FEATURES_AT = [[0], [1], [2], [3], [4], [5], [6], [7]]
LAYER_AT = {5: 1, 6: 2, 7: 3}
SPLIT_AT = {4: [0], 5: [1, 2]}
LAST_SPLIT_AT = {5: [0, 1, 2]}
AHEAD_HI = 4
LAST_PIECES = [(0, 5), (5, 8)]
assert sum(FEATURES_AT, []) == list(range(NO)) and len(FEATURES_AT) == UNITS


def build(nc, ids_gather, ids_onehot, dense, tables, w1, b1, w2, b2, w3, y):
    f32, f32r, i32 = mybir.dt.float32, mybir.dt.float32r, mybir.dt.int32
    ALU = mybir.AluOpType
    ACT = mybir.ActivationFunctionType

    dots_dram = nc.dram_tensor("dots_dram", (BLOCKS, SQ, QUAD, NQ), f32).ap()

    with ExitStack() as ctx:
        def sb(name, shape, dt):
            return ctx.enter_context(nc.sbuf_tensor(name, shape, dt))

        def pb(name, shape):
            return ctx.enter_context(nc.psum_tensor(name, shape, f32))

        def sem(name):
            return ctx.enter_context(nc.semaphore(name))

        tab_hi = sb("tab_hi", [P, NO, CHUNKS, D], f32r)
        tab_lo = sb("tab_lo", [P, NO, CHUNKS, D], f32r)
        emb = sb("emb", [P, 2, BLK, PAD], f32)
        rows = sb("rows", [P, TILES, NG, D], f32)
        idx = sb("idx", [P, 2 * TILES, NG], i32)
        idb = sb("idb", [P, NO, BLK], i32)
        mask = sb("mask", [P, 2, HALF, BLK], f32r)
        dots = sb("dots", [P, 2, FEATURES, NQ], f32)
        zT = sb("zT", [P, 3, BLK], f32)
        z_hi = sb("z_hi", [P, 3, BLK], f32r)
        z_lo = sb("z_lo", [P, 3, BLK], f32r)
        w1_hi = sb("w1_hi", [P, 3, H1], f32r)
        w1_lo = sb("w1_lo", [P, 3, H1], f32r)
        w2_hi = sb("w2_hi", [P, M1, H2], f32r)
        w2_lo = sb("w2_lo", [P, M1, H2], f32r)
        w3_sb = sb("w3_sb", [P, M2], f32)
        b2_sb = sb("b2_sb", [P, M2], f32)
        h1_hi = sb("h1_hi", [P, M1, BLK], f32r)
        h1_lo = sb("h1_lo", [P, M1, BLK], f32r)
        h2 = sb("h2", [P, M2, BLK], f32)
        y_sb = sb("y_sb", [1, BLK], f32)
        ident = sb("ident", [P, P], f32)
        cmp_i = sb("cmp_i", [P, CHUNKS], i32)
        cmp = sb("cmp", [P, CHUNKS], f32)
        late = emb[0:VP, 1, :, :].rearrange("p b s -> p (b s)")
        staged = [late[:, f * CHUNKS * D:(f + 1) * CHUNKS * D] for f in range(NO)]
        w1_staged = dots[:, 1, :, :].rearrange("p j g -> p (j g)")[:, 0:3 * H1].rearrange(
            "p (c n) -> p c n", c=3)
        w2_staged = [zT[:, c, :] for c in range(3)] + [h2[:, 0, :]]

        tile_ps = pb("tile_ps", [P, 512])
        onehot_ps = pb("onehot_ps", [P, 512])
        dots_ps = pb("dots_ps", [P, 2, UNIT_BANKS, 512])
        mlp_ps = pb("mlp_ps", [P, 2, 512])

        table_in = [sem(f"table_in{f}") for f in range(NO)]
        idx_in = [sem(f"idx_in{k}") for k in range(2 * TILES)]
        idb0_in = [sem(f"idb0_in{f}") for f in range(NO)]
        idb_in = [sem(f"idb_in{k}") for k in range(len(IDB_LOADS))]
        weights_in = sem("weights_in")
        gathered = [[sem(f"gathered{q}_{g}") for g in range(NGR)] for q in range(TILES)]
        ident_zeroed = sem("ident_zeroed")
        ident_ready = sem("ident_ready")
        cmp_iota = sem("cmp_iota")
        cmp_ready = sem("cmp_ready")
        hi_ready = sem("hi_ready")
        lo_ready = sem("lo_ready")
        pads_zero = sem("pads_zero")
        mask_ready = sem("mask_ready")
        mask_used = sem("mask_used")
        tile_ps_full = sem("tile_ps_full")
        tile_ps_empty = sem("tile_ps_empty")
        onehot_ps_empty = sem("onehot_ps_empty")
        dots_ps_full = sem("dots_ps_full")
        dots_ps_empty_v = sem("dots_ps_empty_v")
        dots_ps_empty_s = sem("dots_ps_empty_s")
        mlp_ps_full = sem("mlp_ps_full")
        mlp_ps_empty = sem("mlp_ps_empty")
        dots_out = [sem(f"dots_out{k}") for k in range(2)]
        z_in = [sem(f"z_in{c}") for c in range(3)]
        dense_in = sem("dense_in")
        z_split = sem("z_split")
        z_hi_ready = sem("z_hi_ready")
        w1_in = sem("w1_in")
        w1_hi_ready = sem("w1_hi_ready")
        w1_lo_ready = sem("w1_lo_ready")
        w2_hi_ready = sem("w2_hi_ready")
        w2_lo_ready = sem("w2_lo_ready")
        ones_ready = sem("ones_ready")
        h1_hi_ready = sem("h1_hi_ready")
        h1_split = sem("h1_split")
        MLP_CREDIT, DOTS_CREDIT, Y_CREDIT = M2 + 1, 1, 1
        dots_stored = sem("dots_stored")
        y_stored = sem("y_stored")
        y_out = [sem(f"y_out{k}") for k in range(2)]

        block = ctx.enter_context(nc.Block())

        def run_blocks(engine, step):
            step(0, 0, 0)
            with engine.Fori(0, BLOCKS // 2 - 1) as pair:
                step(2 * pair + 1, 1, pair)
                step(2 * pair + 2, 0, pair + 1)
            step(BLOCKS - 1, 1, BLOCKS // 2 - 1)

        def empty_dots(copy, engine, b, parity, u, samples, empty):
            engine.wait_ge(dots_ps_full, UNITS * b + u + 1)
            for s in samples:
                a, z = PAD * s, PAD * (s + 1)
                src = dots_ps[a:z, u % 2, :, 0:QUADS_BANK * QUAD * FEATURES].rearrange(
                    "p a (c t j) -> p a c t j", c=QUADS_BANK, t=QUAD)[:, :, :, s, :]
                dst = dots[a:z, parity, :, u * UNIT_Q:(u + 1) * UNIT_Q].rearrange(
                    "p j (a c) -> p a c j", a=UNIT_BANKS)
                taken = copy(dst, src)
            taken.then_inc(empty, 1)

        def is_int(x, v):
            return isinstance(x, int) and x == v

        @block.sync
        def _(sp):
            sp.sem_inc(dots_stored, DOTS_CREDIT)
            sp.sem_inc(y_stored, Y_CREDIT)

            def load_idx(b, parity):
                for q in range(TILES):
                    k = parity * TILES + q
                    sp.dma_start(idx[:, k, :], ids_gather[:, bass.ds((b * TILES + q) * NG, NG)]
                                 ).then_inc(idx_in[k], 16)

            def load_first_idb(f):
                sp.dma_start(idb[:, f, :],
                             ids_onehot[f:f + 1, 0:BLK].broadcast_to([P, BLK])
                             ).then_inc(idb0_in[f], 16)

            def load_idb(b, k):
                a, z = IDB_LOADS[k].start, IDB_LOADS[k].stop
                sp.dma_start(idb[:, a:z, :],
                             ids_onehot[a:z, bass.ds(b * BLK, BLK)].rearrange("(o f) b -> o f b", o=1
                                                                             ).broadcast_to([P, z - a, BLK])
                             ).then_inc(idb_in[k], 16)

            def store_y(b, parity):
                sp.wait_ge(mlp_ps_empty, MLP_CREDIT * (b + 2))
                sp.dma_start(y[0:1, bass.ds(b * BLK, BLK)], y_sb[0:1, :]).then_inc(y_out[parity], 16)

            def load_weights():
                row = 0
                for c, rows_in in enumerate(K_ROWS[:2] + [BIAS_AT]):
                    sp.dma_start(w1_staged[0:rows_in, c, :], w1[row:row + rows_in, :]).then_inc(w1_in, 16)
                    row += rows_in
                sp.dma_start(w1_staged[BIAS_AT:BIAS_AT + 1, 2, :], b1).then_inc(w1_in, 16)
                for c in range(M1):
                    sp.dma_start(w2_staged[c], w2[c * P:(c + 1) * P, :]).then_inc(weights_in, 16)
                sp.dma_start(w3_sb[:, :], w3).then_inc(weights_in, 16)
                sp.dma_start(b2_sb[:, :], b2).then_inc(weights_in, 16)

            load_idx(0, 0)
            load_first_idb(0)
            for f in range(NO):
                for a, z in ((0, 112), (112, VP)):
                    sp.dma_start(staged[f][a:z, :],
                                 tables[ONEHOT[f]].rearrange("(p c) d -> p (c d)", c=CHUNKS)[a:z, :]
                                 ).then_inc(table_in[f], 16)
                if f < NO - 1:
                    load_first_idb(f + 1)
            load_idx(1, 1)
            load_weights()
            for k, load in enumerate(IDB_LOADS):
                sp.wait_ge(mask_ready, 2 * load.stop)
                load_idb(1, k)

            def step(b, parity, nth):
                last = is_int(b, BLOCKS - 1)
                if not last:
                    for k, load in enumerate(IDB_LOADS):
                        sp.wait_ge(mask_ready, 2 * (NO * (b + 1) + load.stop))
                        load_idb(b + 2, k)
                        if k == 0:
                            sp.wait_ge(tile_ps_full, TILES * NGR * (b + 1))
                            load_idx(b + 2, parity)
                pieces = LAST_PIECES if last else [(0, UNITS)]
                for a, z in pieces:
                    sp.wait_ge(dots_ps_empty_v, UNITS * b + z)
                    sp.wait_ge(dots_ps_empty_s, UNITS * b + z)
                    sp.dma_start(dots_dram[bass.ds(b, 1), :, :, a * UNIT_Q:z * UNIT_Q].rearrange(
                        "o r s g -> s (o r) g"), dots[:, parity, :, a * UNIT_Q:z * UNIT_Q]
                        ).then_inc(dots_out[parity], 16)
                if is_int(b, 0):
                    sp.wait_ge(ones_ready, 1)
                else:
                    sp.wait_ge(z_split, 3 * b)
                sp.dma_start(zT[DENSE_AT:DENSE_AT + DENSE_HALF, 0:2, :],
                             dense[:, bass.ds(b * BLK, BLK)].rearrange("(c p) x -> p c x", c=2)
                             ).then_inc(dense_in, 16)
                sp.wait_ge(dots_out[parity], 16 * (nth + len(pieces)))
                flat = dots_dram[bass.ds(b, 1), 0:STRIDE * 26, :, :].rearrange(
                    "o (i c) s g -> (o i) c (s g)", c=STRIDE)
                for c, (a, z) in enumerate(I_CHUNKS):
                    sp.dma_start(zT[0:(z - a) * KMAX, c, :], flat[a:z, 1:KMAX + 1, :]).then_inc(z_in[c], 16)
                sp.dma_start(zT[FAR_AT:FAR_AT + 13, 2, :], flat[0:13, KMAX + 1, :]).then_inc(z_in[2], 16)
                sp.sem_inc(dots_stored, 1)
                if not is_int(b, 0):
                    store_y(b - 1, 1 - parity)
                    sp.wait_ge(y_out[1 - parity], 16 * (nth + (1 if parity == 1 else 0)))
                    sp.sem_inc(y_stored, 1)

            run_blocks(sp, step)
            store_y(BLOCKS - 1, 1)
            for k in range(2):
                sp.wait_ge(y_out[k], 16 * (BLOCKS // 2))
            for k, load in enumerate(IDB_LOADS):
                sp.wait_ge(idb_in[k], 16 * BLOCKS)
            for q in range(TILES):
                sp.wait_ge(idx_in[q], 16 * (BLOCKS // 2 + 1))

        @block.gpsimd
        def _(pool):
            nc.gpsimd.iota(cmp_i[:, :], pattern=[[1, CHUNKS]], base=0, channel_multiplier=CHUNKS
                           ).then_inc(cmp_iota, 1)
            nc.gpsimd.memset(ident[:, :], 0.0).then_inc(ident_zeroed, 1)
            pool.wait_ge(ident_zeroed, 1)
            nc.gpsimd.affine_select(out=ident[:, :], in_=ident[:, :], compare_op=ALU.not_equal, fill=1.0,
                                    base=0, pattern=[[-1, P]], channel_multiplier=1).then_inc(ident_ready, 1)

            groups_read = pool.alloc_register("groups_read")
            idx_count = [pool.alloc_register(f"idx_count{k}") for k in range(2)]
            pool.reg_mov(groups_read, 1)
            for reg in idx_count:
                pool.reg_mov(reg, 16)

            def step(b, parity, nth):
                for q in range(TILES):
                    k = parity * TILES + q
                    for g, group in enumerate(GROUPS):
                        pool.wait_ge(ident_ready, 1)
                        if g == 0:
                            pool.wait_ge(idx_in[k], idx_count[parity])
                        if not is_int(b, 0):
                            pool.wait_ge(tile_ps_full, groups_read)
                            pool.reg_add(groups_read, groups_read, 1)
                        for r in group:
                            nc.gpsimd.indirect_dma_start(
                                rows[:, q, r, :], None, tables[GATHERED[r]][:, :],
                                bass.IndirectOffsetOnAxis(idx[:, k, r:r + 1], 0)).then_inc(gathered[q][g], 16)
                pool.reg_add(idx_count[parity], idx_count[parity], 16)

            run_blocks(pool, step)

        @block.scalar
        def _(act):
            act.sem_inc(mlp_ps_empty, MLP_CREDIT)

            def empty_onehot(b, parity, v):
                a, z = PAIRS_OH[v].start, PAIRS_OH[v].stop
                act.wait_ge(mask_used, 2 * (NO * b + z))
                nc.scalar.copy(emb[:, parity, :, NG + a:NG + z],
                               onehot_ps[:, 0:(z - a) * BLK].rearrange("p (k b) -> p b k", k=z - a)
                               ).then_inc(onehot_ps_empty, 1)

            def empty_group(b, parity, q, g):
                act.wait_ge(tile_ps_full, NGR * (TILES * b + q) + g + 1)
                k = len(GROUPS[g])
                nc.scalar.copy(emb[:, parity, q * P:(q + 1) * P, GROUPS[g][0]:GROUPS[g][0] + k],
                               tile_ps[:, 0:k * P].rearrange("p (k b) -> p b k", k=k)
                               ).then_inc(tile_ps_empty, 1)

            def empty_next_group(b, parity, q, g, last):
                if q == 0:
                    empty_group(b, parity, 1, g)
                elif not last:
                    empty_group(b + 1, 1 - parity, 0, g)

            def relu1(b):
                for k in range(M1 // 2):
                    act.wait_ge(mlp_ps_full, MLP_STEPS * b + 2 * k + 2)
                    nc.scalar.activation(h1_hi[:, 2 * k:2 * k + 2, :].rearrange("p m b -> p (m b)"),
                                         mlp_ps[:, k, :], ACT.Relu).then_inc(h1_hi_ready, 1)

            def relu2(b):
                for m in range(M2):
                    act.wait_ge(mlp_ps_full, MLP_STEPS * b + M1 + m + 1)
                    nc.scalar.activation(h2[:, m, :], mlp_ps[:, m, 0:BLK], ACT.Relu, bias=b2_sb[:, m:m + 1]
                                         ).then_inc(mlp_ps_empty, 1)

            def empty_y(b):
                act.wait_ge(mlp_ps_full, MLP_STEPS * b + MLP_STEPS)
                nc.scalar.copy(y_sb[0:1, :].rearrange("p (g s) -> p g s", s=QUAD),
                               mlp_ps[0:1, 0, 0:BLK].rearrange("p (s g) -> p g s", s=QUAD)
                               ).then_inc(mlp_ps_empty, 1)

            def split_hi(f):
                act.wait_ge(table_in[f], 32)
                nc.scalar.copy(tab_hi[0:VP, f, :, :].rearrange("p c d -> p (c d)"), staged[f]
                               ).then_inc(hi_ready, 1)

            for f in range(AHEAD_HI):
                split_hi(f)
            for f in range(1, NO):
                if f % 2 == 1 or f == NO - 1:
                    empty_onehot(0, 0, f // 2)
                if f - 1 < NGR:
                    empty_group(0, 0, 0, f - 1)
                if f - 1 + AHEAD_HI < NO:
                    split_hi(f - 1 + AHEAD_HI)
            act.wait_ge(w1_in, 16 * 4)
            for c in range(3):
                moved = nc.scalar.copy(w1_hi[0:K_ROWS[c], c, :], w1_staged[0:K_ROWS[c], c, :])
            moved.then_inc(w1_hi_ready, 1)

            def step(b, parity, nth):
                first, last = is_int(b, 0), is_int(b, BLOCKS - 1)
                act.wait_ge(dots_stored, b)
                for u in range(UNITS):
                    q, i = u // UNITS_TILE, u % UNITS_TILE
                    before, after = GROUPS_AT[i]
                    if first and u == 1:
                        act.wait_ge(weights_in, 16 * (M1 + 2))
                        act.wait_ge(pads_zero, 1)
                        for c in range(M1):
                            moved = nc.scalar.copy(w2_hi[:, c, :], w2_staged[c])
                        moved.then_inc(w2_hi_ready, 1)
                    late = i == UNITS_TILE - 1 and not last
                    if not late:
                        empty_dots(nc.scalar.copy, act, b, parity, u, (2, 3), dots_ps_empty_s)
                    for g in before:
                        empty_next_group(b, parity, q, g, last)
                    for f in FEATURES_AT[u]:
                        if not last and (f % 2 == 1 or f == NO - 1):
                            empty_onehot(b + 1, 1 - parity, f // 2)
                    for g in after:
                        empty_next_group(b, parity, q, g, last)
                    if late:
                        empty_dots(nc.scalar.copy, act, b, parity, u, (2, 3), dots_ps_empty_s)
                    if not first:
                        layer = None if last else LAYER_AT.get(u)
                        if layer == 1:
                            relu1(b - 1)
                        if layer == 2:
                            relu2(b - 1)
                        if layer == 3:
                            act.wait_ge(y_stored, b)
                            empty_y(b - 1)
                if first:
                    act.wait_ge(w1_lo_ready, 1)
                    act.wait_ge(w2_lo_ready, 1)

            run_blocks(act, step)
            relu1(BLOCKS - 2)
            relu2(BLOCKS - 2)
            act.wait_ge(y_stored, BLOCKS - 1)
            empty_y(BLOCKS - 2)
            relu1(BLOCKS - 1)
            relu2(BLOCKS - 1)
            act.wait_ge(y_stored, BLOCKS)
            empty_y(BLOCKS - 1)

        @block.vector
        def _(dve):
            nc.vector.memset(emb[:, 0, :, FEATURES:PAD], 0.0)
            dve.wait_ge(cmp_iota, 1)
            nc.vector.tensor_copy(cmp[:, :], cmp_i[:, :]).then_inc(cmp_ready, 1)
            dve.wait_ge(cmp_ready, 1)

            def masks(b, f):
                if is_int(b, 0):
                    dve.wait_ge(idb0_in[f], 16)
                for k, load in enumerate(IDB_LOADS):
                    if f == load.start and not is_int(b, 0):
                        dve.wait_ge(idb_in[k], 16 * b)
                for h in range(2):
                    n = 2 * (NO * b + f) + h
                    if not (isinstance(n, int) and n < 2):
                        dve.wait_ge(mask_used, n - 1)
                    for c in range(HALF):
                        at = h * HALF + c
                        made = nc.vector.tensor_scalar(mask[0:VP, h, c, :], idb[0:VP, f, :],
                                                       cmp[0:VP, at:at + 1], None, ALU.is_equal)
                    made.then_inc(mask_ready, 1)

            def split_z(b, chunks):
                for c in chunks:
                    if c == 0:
                        dve.wait_ge(dense_in, 16 * (b + 1))
                    dve.wait_ge(z_in[c], (32 if c == 2 else 16) * (b + 1))
                    nc.vector.tensor_copy(z_hi[0:K_ROWS[c], c, :], zT[0:K_ROWS[c], c, :]).then_inc(z_hi_ready, 1)
                    dve.wait_ge(z_hi_ready, 3 * b + c + 1)
                    nc.vector.tensor_tensor(z_lo[0:K_ROWS[c], c, :], zT[0:K_ROWS[c], c, :],
                                            z_hi[0:K_ROWS[c], c, :].bitcast(f32), ALU.subtract
                                            ).then_inc(z_split, 1)

            def split_lo(f):
                dve.wait_ge(hi_ready, f + 1)
                nc.vector.tensor_tensor(
                    tab_lo[0:VP, f, :, :].rearrange("p c d -> p (c d)"), staged[f],
                    tab_hi[0:VP, f, :, :].rearrange("p c d -> p (c d)").bitcast(f32),
                    ALU.subtract).then_inc(lo_ready, 1)

            def split_w1():
                dve.wait_ge(w1_hi_ready, 1)
                for c in range(3):
                    made = nc.vector.tensor_tensor(w1_lo[0:K_ROWS[c], c, :], w1_staged[0:K_ROWS[c], c, :],
                                                   w1_hi[0:K_ROWS[c], c, :].bitcast(f32), ALU.subtract)
                made.then_inc(w1_lo_ready, 1)
                dve.wait_ge(w1_lo_ready, 1)

            def split_w2():
                dve.wait_ge(w2_hi_ready, 1)
                for c in range(M1):
                    made = nc.vector.tensor_tensor(w2_lo[:, c, :], w2_staged[c],
                                                   w2_hi[:, c, :].bitcast(f32), ALU.subtract)
                made.then_inc(w2_lo_ready, 1)
                dve.wait_ge(w2_lo_ready, 1)
                nc.vector.memset(zT[BIAS_AT // 32 * 32:P, 2, :], 1.0).then_inc(ones_ready, 1)

            def split_h1(b):
                for k in range(M1 // 2):
                    dve.wait_ge(h1_hi_ready, M1 // 2 * b + k + 1)
                    lo, hi = [t[:, 2 * k:2 * k + 2, :].rearrange("p m b -> p (m b)") for t in (h1_lo, h1_hi)]
                    nc.vector.scalar_tensor_tensor(lo, mlp_ps[:, k, :], 0.0, hi.bitcast(f32), ALU.max,
                                                   ALU.subtract).then_inc(h1_split, 1)

            masks(0, 0)
            for f in range(NO):
                split_lo(f)
                if f > 0:
                    masks(0, f)
            dve.wait_ge(lo_ready, NO)
            nc.vector.memset(emb[:, 1, :, FEATURES:PAD], 0.0).then_inc(pads_zero, 1)

            def step(b, parity, nth):
                first, last = is_int(b, 0), is_int(b, BLOCKS - 1)
                dve.wait_ge(dots_stored, b)
                for u in range(UNITS):
                    if not last:
                        for f in FEATURES_AT[u]:
                            masks(b + 1, f)
                    empty_dots(nc.vector.tensor_copy, dve, b, parity, u, (0, 1), dots_ps_empty_v)
                    if first and u == 1:
                        split_w1()
                    if first and u == 3:
                        split_w2()
                    if not first:
                        chunks = (LAST_SPLIT_AT if last else SPLIT_AT).get(u)
                        if chunks:
                            split_z(b - 1, chunks)
                        if not last and LAYER_AT.get(u) == 2:
                            split_h1(b - 1)

            run_blocks(dve, step)
            split_h1(BLOCKS - 2)
            split_z(BLOCKS - 1, [0, 1, 2])
            split_h1(BLOCKS - 1)

        @block.tensor
        def _(pe):
            def onehot(b, f):
                if f % 2 == 0 and not (is_int(b, 0) and f == 0):
                    pe.wait_ge(onehot_ps_empty, NPO * b + f // 2)
                out = onehot_ps[:, f % 2 * BLK:(f % 2 + 1) * BLK]
                for h in range(2):
                    pe.wait_ge(mask_ready, 2 * (NO * b + f) + h + 1)
                    for c in range(HALF):
                        at = h * HALF + c
                        nc.tensor.matmul(out, tab_hi[0:VP, f, at, :], mask[0:VP, h, c, :],
                                         start=(at == 0), stop=False)
                        done = nc.tensor.matmul(out, tab_lo[0:VP, f, at, :], mask[0:VP, h, c, :],
                                                start=False, stop=(at == CHUNKS - 1))
                    done.then_inc(mask_used, 1)

            def tile_group(b, q, g):
                n = NGR * (TILES * b + q) + g
                if not is_int(n, 0):
                    pe.wait_ge(tile_ps_empty, n)
                pe.wait_ge(gathered[q][g], 16 * len(GROUPS[g]) * (b + 1))
                for i, r in enumerate(GROUPS[g]):
                    done = nc.tensor.transpose(tile_ps[:, i * P:(i + 1) * P], rows[:, q, r, :], ident[:, :])
                done.then_inc(tile_ps_full, 1)

            def dot_unit(b, parity, u):
                n = UNITS * b + u
                if not (isinstance(n, int) and n < 2):
                    pe.wait_ge(dots_ps_empty_v, n - 1)
                    pe.wait_ge(dots_ps_empty_s, n - 1)
                for i in range(UNIT_Q):
                    at = (u * UNIT_Q + i) * QUAD
                    col = i % QUADS_BANK * QUAD * FEATURES
                    done = nc.tensor.matmul(
                        dots_ps[:, u % 2, i // QUADS_BANK, col:col + QUAD * FEATURES].rearrange(
                            "p (t j) -> p t j", t=QUAD),
                        emb[:, parity, at:at + QUAD, :], emb[:, parity, at:at + QUAD, 0:FEATURES],
                        start=True, stop=True)
                done.then_inc(dots_ps_full, 1)

            def product(out, w_hi, w_lo, x_hi, x_lo, first, last):
                nc.tensor.matmul(out, w_hi, x_hi, start=first, stop=False)
                nc.tensor.matmul(out, w_lo, x_hi, start=False, stop=False)
                return nc.tensor.matmul(out, w_hi, x_lo, start=False, stop=last)

            def layer1(b):
                pe.wait_ge(mlp_ps_empty, MLP_CREDIT * (b + 1))
                for m in range(M1):
                    for c in range(3):
                        if m == 0:
                            pe.wait_ge(z_split, 3 * b + c + 1)
                        k, cols = K_ROWS[c], slice(m * P, (m + 1) * P)
                        done = product(mlp_ps[:, m // 2, m % 2 * BLK:(m % 2 + 1) * BLK],
                                       w1_hi[0:k, c, cols], w1_lo[0:k, c, cols],
                                       z_hi[0:k, c, :], z_lo[0:k, c, :], c == 0, c == 2)
                    done.then_inc(mlp_ps_full, 1)

            def layer2(b):
                for m in range(M2):
                    for c in range(M1):
                        if m == 0 and c % 2 == 0:
                            pe.wait_ge(h1_split, M1 // 2 * b + c // 2 + 1)
                        cols = slice(m * P, (m + 1) * P)
                        done = product(mlp_ps[:, m, 0:BLK], w2_hi[:, c, cols], w2_lo[:, c, cols],
                                       h1_hi[:, c, :], h1_lo[:, c, :], c == 0, c == M1 - 1)
                    done.then_inc(mlp_ps_full, 1)

            def layer3(b):
                for c in range(M2):
                    pe.wait_ge(mlp_ps_empty, MLP_CREDIT * (b + 1) + c + 1)
                    done = nc.tensor.matmul(mlp_ps[0:1, 0, 0:BLK], w3_sb[:, c:c + 1], h2[:, c, :],
                                            start=(c == 0), stop=(c == M2 - 1))
                done.then_inc(mlp_ps_full, 1)

            for f in range(NO):
                pe.wait_ge(lo_ready, f + 1)
                onehot(0, f)
                if f == 1:
                    pe.wait_ge(ident_ready, 1)
                if 0 <= f - 1 < NGR:
                    tile_group(0, 0, f - 1)

            def step(b, parity, nth):
                first, last = is_int(b, 0), is_int(b, BLOCKS - 1)

                def next_tile_group(q, g):
                    if q == 0:
                        tile_group(b, 1, g)
                    elif not last:
                        tile_group(b + 1, 0, g)

                for u in range(UNITS):
                    q, i = u // UNITS_TILE, u % UNITS_TILE
                    if i == 0:
                        pe.wait_ge(tile_ps_empty, NGR * (TILES * b + q + 1))
                        pe.wait_ge(onehot_ps_empty, NPO * (b + 1))
                    before, after = GROUPS_AT[i]
                    late = i == UNITS_TILE - 1 and not last
                    if not late:
                        dot_unit(b, parity, u)
                    for g in before:
                        next_tile_group(q, g)
                    if not last:
                        for f in FEATURES_AT[u]:
                            onehot(b + 1, f)
                    for g in after:
                        next_tile_group(q, g)
                    if late:
                        dot_unit(b, parity, u)
                    if not first:
                        layer = None if last else LAYER_AT.get(u)
                        if layer == 1:
                            layer1(b - 1)
                        if layer == 2:
                            layer2(b - 1)
                        if layer == 3:
                            layer3(b - 1)

                if first:
                    pe.wait_ge(weights_in, 16 * (M1 + 2))
                    pe.wait_ge(w1_lo_ready, 1)
                    pe.wait_ge(w2_lo_ready, 1)
                    pe.wait_ge(pads_zero, 1)

            run_blocks(pe, step)
            layer1(BLOCKS - 2)
            layer2(BLOCKS - 2)
            layer3(BLOCKS - 2)
            layer1(BLOCKS - 1)
            layer2(BLOCKS - 1)
            layer3(BLOCKS - 1)


def pair_column(a, c):
    i, j = min(a, c), max(a, c)
    return j * (j - 1) // 2 + i


def layer1_rows():
    pairs = FEATURES * (FEATURES - 1) // 2

    def pair(row):
        return pair_column(SLOTS[row // FEATURES], SLOTS[row % FEATURES])

    order = []
    for c, (a, z) in enumerate(I_CHUNKS):
        order += [pair(STRIDE * i + k) for i in range(a, z) for k in range(1, KMAX + 1)]
        if c < 2:
            order += [pairs + c * DENSE_HALF + i for i in range(DENSE_HALF)]
    order += [pair(STRIDE * i + KMAX + 1) for i in range(13)]
    return order


def kernel(**inputs):
    import numpy as _np
    import concourse.bacc as _bacc
    from concourse import mybir as _mybir
    from concourse.bass_utils import run_bass_kernel_spmd as _run

    nc = _bacc.Bacc("TRN2", target_bir_lowering=False, num_devices=1,
                     dynamic_dma_scratch_size=DMA_RING)
    ids = _np.asarray(inputs["ids"])
    more_ids = _np.concatenate([ids, ids[:BLK]])
    arrays = {
        "ids_gather": more_ids.reshape(-1, P, FEATURES)[:, :, GATHERED].transpose(1, 0, 2).reshape(P, -1),
        "ids_onehot": more_ids[:, ONEHOT].T,
        "dense": _np.asarray(inputs["dense_ctx"]).reshape(BLOCKS, NQ, QUAD, DENSE).transpose(
            3, 0, 2, 1).reshape(DENSE, BATCH),
        "w1": _np.asarray(inputs["W_top1"])[layer1_rows(), :],
        "b1": _np.asarray(inputs["b_top1"]).reshape(1, H1),
        "w2": _np.asarray(inputs["W_top2"]),
        "b2": _np.asarray(inputs["b_top2"]).reshape(M2, P).T,
        "w3": _np.asarray(inputs["W_top3"]).reshape(M2, P).T,
    }
    for f in range(FEATURES):
        arrays[f"tbl_{f}"] = _np.asarray(inputs[f"tbl_{f}"])
    arrays = {k: _np.ascontiguousarray(v) for k, v in arrays.items()}
    aps = {k: nc.dram_tensor(k, v.shape, _mybir.dt.from_np(v.dtype), kind="ExternalInput").ap()
           for k, v in arrays.items()}
    y = nc.dram_tensor("y", (1, BATCH), _mybir.dt.float32, kind="ExternalOutput").ap()
    build(nc, aps["ids_gather"], aps["ids_onehot"], aps["dense"], [aps[f"tbl_{f}"] for f in range(FEATURES)],
          aps["w1"], aps["b1"], aps["w2"], aps["b2"], aps["w3"], y)
    r = _run(nc, [arrays], core_ids=[0])
    return r.results[0]["y"].reshape(BATCH, 1)
```
